# Optimizing a Trainium2 kernel written in Bass

```python
import numpy as np
import jax
import jax.numpy as jnp

def _softmax(x, axis=-1):
    return jax.nn.softmax(x, axis=axis)
def _gelu(x):
    return jax.nn.gelu(x, approximate=True)
def _silu(x):
    return jax.nn.silu(x)
def _sigmoid(x):
    return jax.nn.sigmoid(x)
def _layernorm(x, axis=-1, eps=1e-5):
    m = jnp.mean(x, axis=axis, keepdims=True)
    v = jnp.var(x, axis=axis, keepdims=True)
    return (x - m) / jnp.sqrt(v + eps)
def _scatter_add(tgt, idx, src, axis=0):
    return tgt.at[idx].add(src)
def _segment_sum(src, seg, n):
    return jax.ops.segment_sum(src, seg, n)

kernel_name = 'mk_adj_resnorm_d1_adj_512_f7b6cd'

def setup_inputs(seed: int = 0):
    np.random.seed(seed)
    _w = jnp.asarray
    def _rec_inputs():
        import jax
        import jax.numpy as jnp
        _gk = jax.random.key(seed)
        x = 7.34e-05 + 1 * jax.random.normal(jax.random.fold_in(_gk, 1), (16, 1024, 512), jnp.float32)
        _a = jax.random.bernoulli(jax.random.fold_in(_gk, 2), 0.03125, (1024, 1024))
        _a = jnp.logical_or(_a, jnp.swapaxes(_a, -1, -2))
        _a = jnp.logical_or(_a, jnp.eye(1024, dtype=bool))
        _af = _a.astype(jnp.float32)
        adj = _af
        return x, adj
    x, adj = _rec_inputs()
    def _L0_gnn_setup():
        import jax, jax.numpy as jnp
        import numpy as np
        B, N, D, H = (16, 1025, 512, 8)
        LN_EPS = 1e-05

        def _make_mask(key, n):
            n_proto = n - 1
            adj = jax.random.bernoulli(key, 0.03, (n_proto, n_proto)).astype(jnp.float32)
            adj = jnp.clip(adj + adj.T + jnp.eye(n_proto, dtype=jnp.float32), 0.0, 1.0)
            mask = jnp.zeros((n, n), dtype=jnp.float32)
            mask = mask.at[0, :].set(1.0).at[:, 0].set(1.0)
            mask = mask.at[1:, 1:].set(adj)
            return mask
        key = jax.random.key(seed)
        ks = jax.random.split(key, 7)
        s = 1.0 / np.sqrt(D)
        return {'x': jax.random.normal(ks[0], (B, N, D), dtype=jnp.float32), 'w_qkv': jax.random.uniform(ks[1], (D, 3 * D), dtype=jnp.float32, minval=-s, maxval=s), 'w_proj': jax.random.uniform(ks[2], (D, D), dtype=jnp.float32, minval=-s, maxval=s), 'b_proj': jnp.zeros((D,), dtype=jnp.float32), 'ln_gamma': jnp.ones((D,), dtype=jnp.float32), 'ln_beta': jnp.zeros((D,), dtype=jnp.float32), 'attn_mask': _make_mask(ks[3], N)}
    _L0_gnn_all = _L0_gnn_setup()
    _L0_gnn_in = {k: v for k, v in _L0_gnn_all.items() if k in ('w_qkv', 'w_proj', 'b_proj', 'ln_gamma', 'ln_beta', )}
    del _L0_gnn_all

    return {
        "x": x,
        "adj": adj,
        "L0_gnn_w_qkv": _L0_gnn_in["w_qkv"],
        "L0_gnn_w_proj": _L0_gnn_in["w_proj"],
        "L0_gnn_b_proj": _L0_gnn_in["b_proj"],
        "L0_gnn_ln_gamma": _L0_gnn_in["ln_gamma"],
        "L0_gnn_ln_beta": _L0_gnn_in["ln_beta"],
    }

def reference(x, adj, L0_gnn_w_qkv, L0_gnn_w_proj, L0_gnn_b_proj, L0_gnn_ln_gamma, L0_gnn_ln_beta):
    import jax
    import jax.numpy as jnp
    def _L0_gnn_ref(x, w_qkv, w_proj, b_proj, ln_gamma, ln_beta, attn_mask):
        import jax, jax.numpy as jnp
        import numpy as np
        B, N, D, H = (16, 1025, 512, 8)
        LN_EPS = 1e-05

        def _make_mask(key, n):
            n_proto = n - 1
            adj = jax.random.bernoulli(key, 0.03, (n_proto, n_proto)).astype(jnp.float32)
            adj = jnp.clip(adj + adj.T + jnp.eye(n_proto, dtype=jnp.float32), 0.0, 1.0)
            mask = jnp.zeros((n, n), dtype=jnp.float32)
            mask = mask.at[0, :].set(1.0).at[:, 0].set(1.0)
            mask = mask.at[1:, 1:].set(adj)
            return mask
        b, n, d = x.shape
        hd = d // H
        scale = hd ** (-0.5)
        qkv = (x @ w_qkv).reshape(b, n, 3, H, hd).transpose(2, 0, 3, 1, 4)
        q, k, v = (qkv[0], qkv[1], qkv[2])
        attn = jnp.einsum('bhnd,bhmd->bhnm', q, k) * scale
        attn = jnp.where(attn_mask[None, None] == 0, -jnp.inf, attn)
        attn = jax.nn.softmax(attn, axis=-1)
        o = jnp.einsum('bhnm,bhmd->bhnd', attn, v).transpose(0, 2, 1, 3).reshape(b, n, d)
        o = o @ w_proj + b_proj
        mu = jnp.mean(o, axis=-1, keepdims=True)
        var = jnp.mean(jnp.square(o - mu), axis=-1, keepdims=True)
        ln = (o - mu) * jax.lax.rsqrt(var + LN_EPS) * ln_gamma + ln_beta
        return o + ln

    x = _layernorm(x + _L0_gnn_ref(x, L0_gnn_w_qkv, L0_gnn_w_proj, L0_gnn_b_proj, L0_gnn_ln_gamma, L0_gnn_ln_beta, adj), axis=-1)
    return x


_drawn_inputs = setup_inputs


def setup_inputs(seed=0):
    import zlib

    import numpy as np

    out = dict(_drawn_inputs(seed))
    spreads = {'L0_gnn_b_proj': (0.0, 0.1), 'L0_gnn_ln_gamma': (1.0, 0.2), 'L0_gnn_ln_beta': (0.0, 0.1)}
    factors = {}
    for name, (base, spread) in spreads.items():
        noise = np.random.default_rng([zlib.crc32(name.encode()), seed]).standard_normal(out[name].shape)
        drawn = base * np.exp(spread * noise) if base else spread * noise
        out[name] = jnp.asarray(drawn.astype(out[name].dtype))
    for name, factor in factors.items():
        out[name] = (out[name] * factor).astype(out[name].dtype)
    return out
```

```python
from contextlib import ExitStack

import concourse.bass as bass
from concourse import mybir

F32, F16, BF16 = mybir.dt.float32, mybir.dt.float16, mybir.dt.bfloat16
ALU = mybir.AluOpType
ACT = mybir.ActivationFunctionType

P = 128
B, N, D, H = 16, 1024, 512, 8
HD = D // H
T = N // P
KC = D // P
CH = 512
STEPS = 2 * H
SLOTS = T
UNITS = STEPS * SLOTS
LAG = 2
VW = HD + 1 + HD
VP = VW + 1
WSCALE = 256.0
UNSCALE = 1.0 / WSCALE
SCALE = HD ** -0.5
NEG = -1.0e30
EPS = 1e-5

NXT, CUR, PRV = "next", "current", "previous"
TURNS = {
    0: [("QK", 5, CUR), ("QK", 6, CUR), ("OT", 6, PRV), ("OT", 7, PRV)],
    1: [("QK", 7, CUR), ("PJ", 0, PRV)],
    2: [("PJ", 1, PRV), ("QK", 8, CUR)],
    3: [("PJ", 2, PRV), ("QK", 9, CUR)],
    4: [("PJ", 3, PRV), ("QK", 10, CUR)],
    5: [("PJ", 4, PRV), ("QK", 11, CUR)],
    6: [("PJ", 5, PRV), ("QK", 12, CUR)],
    7: [("PJ", 6, PRV), ("QK", 13, CUR)],
    8: [("PJ", 7, PRV), ("QK", 14, CUR), ("OT", 0, CUR), ("OT", 1, CUR)],
    9: [("QK", 15, CUR), ("OT", 2, CUR), ("OT", 3, CUR)],
    10: [("XT", t, NXT) for t in range(T)],
    11: [("QK", 0, NXT), ("QK", 1, NXT)],
    12: [("QK", 2, NXT), ("QK", 3, NXT)],
    13: [("OT", 4, CUR), ("OT", 5, CUR), ("V", 0, NXT), ("V", 1, NXT), ("V", 2, NXT)],
    14: [("V", 3, NXT), ("V", 4, NXT), ("V", 5, NXT)],
    15: [("V", 6, NXT), ("V", 7, NXT), ("QK", 4, NXT)],
}
STACK_AT = {0: [4], 1: [5, 6], 2: [7], 4: [8, 9], 5: [10], 6: [11], 8: [12, 13], 9: [14], 10: [15],
            12: [0, 1], 13: [2, 3]}
MATMULS = {"XT": KC, "OT": T // 2, "QK": 3 * KC, "V": 3 * KC, "PJ": 3 * KC}


def active(b, whose):
    if not isinstance(b, int):
        return True
    return {NXT: b < B - 1, CUR: 0 <= b < B, PRV: b >= 1}[whose]


def turn_numbers(b, vector_only):
    def listed(body):
        return [t for s in range(STEPS) for t in TURNS[s]
                if active(body, t[2]) and not (vector_only and t[0] == "PJ")]
    if isinstance(b, int):
        before = sum(len(listed(x)) for x in range(-1, b))
    else:
        full = len([t for s in range(STEPS) for t in TURNS[s] if not (vector_only and t[0] == "PJ")])
        before = b * full + (len(listed(-1)) + len(listed(0)) - full)
    return {t: (before, i) for i, t in enumerate(listed(b))}


def plus(pair, k):
    return pair[0] + (pair[1] + k)


def parity(b, turn):
    if isinstance(b, int):
        before, i = turn_numbers(b, False)[turn]
        return (before + i) % 2
    before, i = turn_numbers(1, False)[turn]
    return (before + i) % 2


def slot_items(b, s, j):
    items = [(t, i) for t in TURNS[s] for i in range(MATMULS[t[0]])]
    n = len(items)
    return [(t, i) for t, i in items[n * j // SLOTS:n * (j + 1) // SLOTS] if active(b, t[2])]


def turns_ending(b, s, j):
    return [t for t, i in slot_items(b, s, j) if i == MATMULS[t[0]] - 1]


def owner(b, whose):
    return {NXT: b + 1, CUR: b, PRV: b - 1}[whose]


def wait(eng, sem, value):
    if isinstance(value, int) and value <= 0:
        return
    eng.wait_ge(sem, value)


def wait_alone(eng, sem, value):
    wait(eng, sem, value)
    eng.nop(nofuse=True)


def attention_block(nc, x, adj, w_qkv, w_proj, b_proj, gamma, beta, out):
    x_tiles = x.rearrange("b (t p) d -> (b t) p d", p=P)
    out_tiles = out.rearrange("b (t p) d -> (b t) p d", p=P)
    with ExitStack() as ctx:
        def sb(name, shape, dt):
            return ctx.enter_context(nc.sbuf_tensor(name, shape, dt))

        def sem(name):
            return ctx.enter_context(nc.semaphore(name))

        def sems(name, n):
            return [sem(f"{name}{i}") for i in range(n)]

        mask_q = sb("mask_q", [P, T, N], BF16)
        mask_k = sb("mask_k", [P, T, N], BF16)
        w_hi = sb("w_hi", [P, KC, 3 * D], F16)
        w_lo = sb("w_lo", [P, KC, 3 * D], F16)
        wp_hi = sb("wp_hi", [P, KC, D], F16)
        wp_lo = sb("wp_lo", [P, KC, D], F16)
        xt_hi = sb("xt_hi", [P, KC, N], F16)
        xt_lo = sb("xt_lo", [P, KC, N], F16)
        x_nat = sb("x_nat", [P, 4, D], F32)
        qk_hi = sb("qk_hi", [P, 4, CH], F16)
        qk_lo = sb("qk_lo", [P, 4, CH], F16)
        stack = sb("stack", [P, 2, 2, 4, N], F16)
        K_A, K_B, Q_A, Q_B = range(4)
        v_live = sb("v_live", [P, H, T, VP], F16)
        v_next = sb("v_next", [P, 2, T, VP], F16)
        p32 = sb("p32", [P, 4, CH], F32)
        p_hi = sb("p_hi", [P, 4, CH], F16)
        p_lo = sb("p_lo", [P, 4, CH], F16)
        o_pair = sb("o_pair", [P, 2, T, P], F32)
        ot_hi = sb("ot_hi", [P, KC, N], F16)
        ot_lo = sb("ot_lo", [P, KC, N], F16)
        c_max = sb("c_max", [P, 2, 4], F32)
        c_neg = sb("c_neg", [P, 2, 8], F16)
        c_row = sb("c_row", [8, 2, P], F16)
        recip = sb("recip", [P, 2, 4], F32)
        x_res = sb("x_res", [P, 2, D], F32)
        y = sb("y", [P, 2, D], F32)
        ln_o = sb("ln_o", [P, D], F32)
        stats = sb("stats", [P, 2, 6], F32)
        mv = sb("mv", [P, 2, 3], F32)
        norm = sb("norm", [P, 2, 2], F32)
        minus_half = sb("minus_half", [P, 1], F32)
        gamma_b = sb("gamma_b", [P, D], F32)
        beta_b = sb("beta_b", [P, D], F32)
        bias_b = sb("bias_b", [P, D], F32)
        ident = sb("ident", [P, P], F32)
        ident_bf = sb("ident_bf", [P, P], BF16)
        ident_h = sb("ident_h", [P, P], F16)
        staging = stack[:, :, :, :, :].rearrange("p a b c n -> p (a b c n)").bitcast(F32)
        w_in = staging[:, 0:KC * 3 * D].rearrange("p (k n) -> p k n", k=KC)
        wp_in = staging[:, 0:KC * D].rearrange("p (k n) -> p k n", k=KC)
        adj_in = staging[:, KC * 3 * D:KC * 3 * D + 2 * N].rearrange("p (a n) -> p a n", a=2)

        def pb(name):
            return ctx.enter_context(nc.psum_tensor(name, [P, CH], F32))

        st_bank = [pb(f"st_bank{i}") for i in range(2)]
        sm_both = ctx.enter_context(nc.psum_tensor("sm_both", [P, 2 * CH], F32))
        pv_bank = [pb(f"pv_bank{i}") for i in range(2)]
        side = [pb(f"side{i}") for i in range(2)]

        w_loaded, wp_loaded, const_loaded = sem("w_loaded"), sem("wp_loaded"), sem("const_loaded")
        adj_loaded = sems("adj_loaded", 2)
        ident_zero, ident_ready, constants_set = sem("ident_zero"), sem("ident_ready"), sem("constants_set")
        half_set = sem("half_set")
        w_hi_ready, w_ready = sem("w_hi_ready"), sem("w_ready")
        mask_q_ready, mask_t_ready, mask_k_ready = sem("mask_q_ready"), sem("mask_t_ready"), sem("mask_k_ready")
        x_loaded = sems("x_loaded", 4)
        k_in = sems("k_in", 2)
        q_in = [sems(f"q_in{i}_", 2) for i in range(2)]
        c_in = sems("c_in", 2)
        v_in = sems("v_in", 2)
        st_ready = sem("st_ready")
        exp32_done, exp16_done, lo_done = sem("exp32_done"), sem("exp16_done"), sem("lo_done")
        pv_done = sem("pv_done")
        o_done = sem("o_done")
        recip_done = sem("recip_done")
        sm_ready, max_done = sem("sm_ready"), sem("max_done")
        c_hi_done, c_done, ct_ready, c_row_ready = sem("c_hi_done"), sem("c_done"), sem("ct_ready"), sem("c_row_ready")
        side_ready, side_act, side_dve = sem("side_ready"), sem("side_act"), sem("side_dve")
        xr_loaded, stored = sems("xr_loaded", 2), sems("stored", 2)
        o_biased, xr_biased, sum1_done, ln_scaled, sum2_done = (
            sem("o_biased"), sem("xr_biased"), sem("sum1_done"), sem("ln_scaled"), sem("sum2_done"))
        stat_a, stat_b = sem("stat_a"), sem("stat_b")
        sigma_a, sigma_b = sem("sigma_a"), sem("sigma_b")
        norm_ready = sems("norm_ready", 2)
        ln_ready, out_ready = sem("ln_ready"), sem("out_ready")

        block = ctx.enter_context(nc.Block())

        def bodies(eng, body):
            body(-1)
            body(0)
            with eng.Fori(1, B - 1) as b:
                body(b)
            body(B - 1)
            body(B)

        def fills(batch, pair):
            return batch * 2 + (pair // 2 + 1)

        def max_target(b, s):
            return (b, s + 2) if s + 2 < STEPS else (b + 1, s + 2 - STEPS)

        def row_target(b, s):
            return (b, s + 1) if s + 1 < STEPS else (b + 1, 0)

        def is_batch(b):
            return not isinstance(b, int) or 0 <= b < B

        def pv_unit(b, s, j):
            k = s * SLOTS + j - LAG
            return (b, k) if k >= 0 else (b - 1, k + UNITS)

        @block.sync
        def _(sp):
            for kc in range(KC):
                sp.dma_start(w_in[:, kc, :], w_qkv[kc * P:(kc + 1) * P, :]).then_inc(w_loaded, 16)
            for t in range(T):
                if t >= 2:
                    sp.wait_ge(mask_q_ready, t - 1)
                sp.dma_start(adj_in[:, t % 2, :], adj[t * P:(t + 1) * P, :]).then_inc(adj_loaded[t % 2], 16)
            for dst, src in ((gamma_b, gamma), (beta_b, beta), (bias_b, b_proj)):
                sp.dma_start(dst[:, :], src.rearrange("(o n) -> o n", o=1).broadcast_to([P, D])).then_inc(const_loaded, 16)
            sp.wait_ge(w_ready, 2 * KC)
            for kc in range(KC):
                sp.dma_start(wp_in[:, kc, :], w_proj[kc * P:(kc + 1) * P, :]).then_inc(wp_loaded, 16)

            def fill_stack(b, s, g):
                whose = NXT if g < 5 and s >= 11 else CUR
                turn = ("QK", g, NXT if g < 5 else CUR)
                made_in = b - 1 if g == 4 else b
                if not active(b, whose):
                    return
                batch = owner(b, whose)
                pair, part = g // 4, g % 4
                sl = pair % 2
                wait_alone(sp, side_dve, plus(turn_numbers(made_in, True)[turn], 1))
                wait(sp, st_ready, batch * UNITS + 32 * (pair - 1))
                for ph in range(2):
                    rows = slice(ph * HD, (ph + 1) * HD)
                    cols = slice((part % 2) * CH, (part % 2 + 1) * CH)
                    hi, lo = qk_hi[rows, g % 4, :], qk_lo[rows, g % 4, :]
                    if part < 2:
                        done = k_in[sl]
                        moves = ((K_A, 0, hi), (K_B, 0, hi), (K_A, HD, lo))
                    else:
                        done = q_in[sl][part % 2]
                        moves = ((Q_A, 0, hi), (Q_A, HD, hi), (Q_B, 0, lo))
                    for what, row, src in moves:
                        sp.dma_start(stack[row:row + HD, sl, ph, what, cols], src).then_inc(done, 16)

            def load_x(b, t):
                if active(b, NXT):
                    if t >= 4:
                        wait_alone(sp, side_ready, plus(turn_numbers(b, False)[("XT", t - 4, NXT)], 1))
                    elif is_batch(b):
                        wait_alone(sp, side_ready, plus(turn_numbers(b - 1, False)[("XT", t + 4, NXT)], 1))
                    sp.dma_start(x_nat[:, t % 4, :], x_tiles[(b + 1) * T + t, :, :]).then_inc(x_loaded[t % 4], 16)

            def body(b):
                for s in range(STEPS):
                    for g in STACK_AT.get(s, ()):
                        fill_stack(b, s, g)
                    if s == 1 and is_batch(b):
                        sp.wait_ge(side_dve, plus(turn_numbers(b - 1, True)[("V", T - 1, NXT)], 1))
                        wait(sp, pv_done, b * UNITS)
                        for hh in range(2):
                            sp.dma_start(v_live[:, H - 2 + hh, :, :], v_next[:, hh, :, :]).then_inc(v_in[hh], 16)
                    if s == 12 and active(b, PRV):
                        for i in range(2):
                            wait_alone(sp, stored[i], b * 64)
                    if s == 9:
                        for t in range(4):
                            load_x(b, t)
                    for j in range(SLOTS):
                        if s == 10 and j < 4:
                            load_x(b, j + 4)
                        tb, ts = row_target(b, s)
                        if j == 4 and is_batch(tb):
                            h, qc = ts // 2, ts % 2
                            wait_alone(sp, c_row_ready, tb * STEPS + (ts + 1))
                            wait(sp, st_ready, tb * UNITS + (ts - 7) * SLOTS)
                            sp.dma_start(stack[HD:HD + 2, (h // 2) % 2, h % 2, Q_B, qc * CH:(qc + 1) * CH],
                                         c_row[:, ts % 2, :]).then_inc(c_in[ts % 2], 16)
                        if active(b, PRV):
                            n0 = b * T - T
                            t = s - 3
                            if j == 6 and 0 <= t < T:
                                wait_alone(sp, out_ready, n0 + (t + 1))
                                sp.dma_start(out_tiles[n0 + t, :, :], x_res[:, t % 2, :]).then_inc(stored[t % 2], 16)
                            t = s - 1
                            if j == 7 and 0 <= t < T:
                                if t >= 2:
                                    wait_alone(sp, stored[t % 2], b * 64 + (t // 2 * 16 - 64))
                                sp.dma_start(x_res[:, t % 2, :], x_tiles[n0 + t, :, :]).then_inc(xr_loaded[t % 2], 16)

            bodies(sp, body)
            for i in range(2):
                sp.wait_ge(stored[i], 16 * B * T // 2)

        @block.tensor
        def _(pe):
            pe.wait_ge(ident_ready, 3)
            for qt in range(T):
                pe.wait_ge(mask_q_ready, qt + 1)
                if qt >= 2:
                    pe.wait_ge(mask_k_ready, qt - 1)
                bank = st_bank[qt % 2][:, :].bitcast(BF16)
                for kt in range(T):
                    last = nc.tensor.transpose(bank[:, kt * P:(kt + 1) * P], mask_q[:, qt, kt * P:(kt + 1) * P],
                                               ident_bf[:, :])
                last.then_inc(mask_t_ready, 1)
            pe.wait_ge(mask_k_ready, T)
            pe.wait_ge(w_ready, 2 * KC + 2 * KC)
            pe.wait_ge(constants_set, 6)

            def side_matmul(b, turn, i):
                kind, idx, whose = turn
                bank = side[parity(b, turn)]
                batch = owner(b, whose)
                if i == 0:
                    number = turn_numbers(b, False)[turn]
                    wait(pe, side_act, plus(number, -1))
                    all_turns = list(turn_numbers(b, False))
                    at = all_turns.index(turn)
                    dve = turn_numbers(b, True)
                    before = len([t for t in all_turns[:at] if t[0] != "PJ"])
                    behind = 0 if at and all_turns[at - 1][0] == "PJ" else 1
                    base = next(iter(dve.values()))[0] if dve else 0
                    wait(pe, side_dve, base + (before - behind))
                k, part = i // 3, i % 3
                if kind == "XT":
                    if i == 0:
                        pe.wait_ge(x_loaded[idx % 4], batch * 32 + (idx // 4 + 1) * 16)
                    mm = nc.tensor.transpose(bank[:, i * P:(i + 1) * P], x_nat[:, idx % 4, i * P:(i + 1) * P], ident[:, :])
                elif kind == "OT":
                    pair, half = idx // 2, idx % 2
                    if i == 0:
                        pe.wait_ge(o_done, batch * STEPS + 4 * (pair + 1))
                    mm = nc.tensor.transpose(bank[:, i * P:(i + 1) * P], o_pair[:, pair % 2, half * 4 + i, :], ident[:, :])
                elif kind == "QK":
                    if i == 0 and idx == 0:
                        pe.wait_ge(side_dve, plus(turn_numbers(b, True)[("XT", T - 1, NXT)], 1))
                    g = idx % 4
                    col = (idx // 4) * P + (D if g < 2 else 0)
                    w = (w_hi, w_hi, w_lo)[part]
                    xt = (xt_hi, xt_lo, xt_hi)[part]
                    mm = nc.tensor.matmul(bank[:, :], w[:, k, col:col + P], xt[:, k, (g % 2) * CH:(g % 2 + 1) * CH],
                                          start=(i == 0), stop=(i == 3 * KC - 1))
                else:
                    if kind == "V":
                        rows, w, cols = (xt_hi, xt_lo, xt_hi)[part], (w_hi, w_hi, w_lo)[part], slice(2 * D, 3 * D)
                    else:
                        rows, w, cols = (ot_hi, ot_lo, ot_hi)[part], (wp_hi, wp_hi, wp_lo)[part], slice(0, D)
                        if i == 0 and idx == 0:
                            pe.wait_ge(side_dve, plus(turn_numbers(b, True)[("OT", 7, PRV)], 1))
                    mm = nc.tensor.matmul(bank[:, :], rows[:, k, idx * P:(idx + 1) * P], w[:, k, cols],
                                          start=(i == 0), stop=(i == 3 * KC - 1))
                if i == MATMULS[kind] - 1:
                    mm.then_inc(side_ready, 1)

            def scores_t(b, s, j):
                h, qc = s // 2, s % 2
                q = slice(qc * CH, (qc + 1) * CH)
                keys = slice(j * P, (j + 1) * P)
                st = stack[:, (h // 2) % 2, h % 2, :, :]
                if j == 0:
                    pe.wait_ge(c_in[s % 2], b * (16 * 8) + (s // 2 + 1) * 16)
                bank = st_bank[j % 2]
                wait(pe, exp16_done, b * UNITS + (s * SLOTS + j - 1))
                nc.tensor.matmul(bank[:, :], st[:, K_A, keys], st[:, Q_A, q], start=True, stop=False)
                nc.tensor.matmul(bank[:, :], st[:, K_B, keys], st[:, Q_B, q], start=False, stop=False)
                nc.tensor.matmul(bank[:, :], ident_bf[:, :], mask_k[:, j, q], start=False, stop=True
                                 ).then_inc(st_ready, 1)

            def times_v(b, s, j):
                ub, u = pv_unit(b, s, j)
                if not is_batch(ub):
                    return
                us, kt = u // SLOTS, u % SLOTS
                h = us // 2
                bank = pv_bank[us % 2]
                pe.wait_ge(lo_done, ub * UNITS + (u + 1))
                if kt == 0:
                    wait(pe, o_done, ub * STEPS + (us - 1))
                    pe.wait_ge(c_row_ready, ub * STEPS + (us + 1))
                    if us == 0:
                        pe.wait_ge(side_dve, plus(turn_numbers(b - 1, True)[("V", T - 1, NXT)], 1))
                    if us in (2 * (H - 2), 2 * (H - 1)):
                        pe.wait_ge(v_in[h - (H - 2)], ub * 16 + 16)
                for t in range(4):
                    o = bank[:, t * (HD + 1):(t + 1) * (HD + 1)]
                    hi = p_hi[:, u % 4, t * P:(t + 1) * P]
                    lo = p_lo[:, u % 4, t * P:(t + 1) * P]
                    v = v_live[:, h, kt, :]
                    nc.tensor.matmul(o, hi, v[:, 0:HD + 1], start=(kt == 0 and t == 0), stop=False, skip_group_check=True)
                    nc.tensor.matmul(o[:, 0:HD], hi, v[:, HD + 1:VW], start=False, stop=False, skip_group_check=True)
                    mm = nc.tensor.matmul(o, lo, v[:, 0:HD + 1], start=False, stop=(kt == SLOTS - 1), skip_group_check=True)
                mm.then_inc(pv_done, 1)

            def scores_for_max(b, s, j):
                tb, ts = max_target(b, s)
                if not is_batch(tb):
                    return
                h, qc = ts // 2, ts % 2
                qt = qc * 4 + j // 2
                pair = h // 2
                if j == 0 and ts % 4 == 0:
                    pe.wait_ge(k_in[pair % 2], tb * (2 * 192) + (pair // 2 + 1) * 192)
                if j == 0 and ts % 4 < 2:
                    pe.wait_ge(q_in[pair % 2][qc], tb * (2 * 96) + (pair // 2 + 1) * 96)
                if j % 2 == 0:
                    wait(pe, max_done, tb * (STEPS * 4) + (ts * 4 + j // 2))
                st = stack[:, pair % 2, h % 2, :, :]
                mm = nc.tensor.matmul(sm_both[:, (j % 2) * CH:(j % 2 + 1) * CH], st[:, Q_A, qt * P:(qt + 1) * P],
                                      st[:, K_A, (j % 2) * CH:(j % 2 + 1) * CH], start=True, stop=True)
                if j % 2:
                    mm.then_inc(sm_ready, 1)

            def transpose_c(b, s):
                tb, ts = row_target(b, s)
                if not is_batch(tb):
                    return
                pe.wait_ge(c_done, tb * STEPS + (ts + 1))
                wait(pe, o_done, tb * STEPS + (ts - 1))
                nc.tensor.transpose(pv_bank[ts % 2][:, :].bitcast(F16)[0:8, 0:P], c_neg[:, ts % 2, :], ident_h[:, :]
                                    ).then_inc(ct_ready, 1)

            def body(b):
                for s in range(STEPS):
                    for j in range(SLOTS):
                        if j % 2:
                            scores_for_max(b, s, j)
                        if active(b, CUR):
                            scores_t(b, s, j)
                        times_v(b, s, j)
                        for turn, i in slot_items(b, s, j):
                            side_matmul(b, turn, i)
                        if j % 2 == 0:
                            scores_for_max(b, s, j)
                        if j == 4:
                            transpose_c(b, s)

            bodies(pe, body)

        @block.scalar
        def _(act):
            act.wait_ge(w_loaded, 16 * KC)
            for kc in range(KC):
                nc.scalar.activation(w_hi[:, kc, :], w_in[:, kc, :], ACT.Copy, scale=WSCALE).then_inc(w_hi_ready, 1)
            for qt in range(T):
                act.wait_ge(mask_t_ready, qt + 1)
                nc.scalar.activation(mask_k[:, :, qt * P:(qt + 1) * P],
                                     st_bank[qt % 2][:, :].bitcast(BF16).rearrange("p (k q) -> p k q", k=T),
                                     ACT.Copy).then_inc(mask_k_ready, 1)
            act.wait_ge(wp_loaded, 16 * KC)
            for kc in range(KC):
                nc.scalar.activation(wp_hi[:, kc, :], wp_in[:, kc, :], ACT.Copy, scale=WSCALE).then_inc(w_hi_ready, 1)

            act.wait_ge(ident_ready, 5)

            def side_out(b, turn):
                kind, idx, whose = turn
                batch = owner(b, whose)
                bank = side[parity(b, turn)]
                act.wait_ge(side_ready, plus(turn_numbers(b, False)[turn], 1))
                if kind == "XT":
                    nc.scalar.activation(xt_hi[:, :, idx * P:(idx + 1) * P], bank[:, :].rearrange("p (k q) -> p k q", k=KC),
                                         ACT.Copy).then_inc(side_act, 1)
                elif kind == "OT":
                    nc.scalar.activation(ot_hi[:, idx // 2, (idx % 2) * CH:(idx % 2 + 1) * CH], bank[:, :],
                                         ACT.Copy).then_inc(side_act, 1)
                elif kind == "QK":
                    pair, part = idx // 4, idx % 4
                    sl = (pair + 1) % 2
                    filled = batch * 2 + (pair - 1) // 2 + 1 if pair else batch * 2
                    if part < 2:
                        wait(act, k_in[sl], filled * 192)
                    else:
                        wait(act, q_in[sl][part % 2], filled * 96)
                    nc.scalar.activation(qk_hi[:, idx % 4, :], bank[:, :], ACT.Copy, scale=UNSCALE).then_inc(side_act, 1)
                elif kind == "V":
                    heads = bank[:, :].rearrange("p (h d) -> p h d", h=H)
                    if idx == 0:
                        wait(act, pv_done, b * UNITS + (H - 2) * 2 * SLOTS)
                        for hh in range(2):
                            wait(act, v_in[hh], batch * 16)
                    nc.scalar.activation(v_live[:, 0:H - 2, idx, 0:HD], heads[:, 0:H - 2, :], ACT.Copy, scale=UNSCALE)
                    nc.scalar.activation(v_next[:, :, idx, 0:HD], heads[:, H - 2:H, :], ACT.Copy, scale=UNSCALE
                                         ).then_inc(side_act, 1)
                else:
                    if idx >= 2:
                        act.wait_ge(sum1_done, batch * T + (idx - 1))
                        act.wait_ge(ln_ready, batch * T + (idx - 1))
                    nc.scalar.activation(y[:, idx % 2, :], bank[:, :], ACT.Copy, scale=UNSCALE).then_inc(side_act, 1)

            def body(b):
                for s in range(STEPS):
                    for j in range(SLOTS):
                        if active(b, CUR):
                            u = s * SLOTS + j
                            act.wait_ge(st_ready, b * UNITS + (u + 1))
                            wait(act, lo_done, b * UNITS + (u - 3))
                            nc.scalar.activation(p32[:, u % 4, :], st_bank[j % 2][:, :], ACT.Exp, scale=SCALE
                                                 ).then_inc(exp32_done, 1)
                            wait(act, pv_done, b * UNITS + (u - 3))
                            nc.scalar.activation(p_hi[:, u % 4, :], st_bank[j % 2][:, :], ACT.Exp, scale=SCALE
                                                 ).then_inc(exp16_done, 1)
                        for turn in turns_ending(b, s, j):
                            side_out(b, turn)
                        tb, ts = row_target(b, s)
                        if j == 4 and is_batch(tb):
                            act.wait_ge(ct_ready, tb * STEPS + (ts + 1))
                            wait(act, c_in[ts % 2], tb * (16 * 8) + (ts // 2) * 16)
                            nc.scalar.activation(c_row[:, ts % 2, :], pv_bank[ts % 2][:, :].bitcast(F16)[0:8, 0:P],
                                                 ACT.Copy).then_inc(c_row_ready, 1)
                        if active(b, PRV):
                            n0 = b * T - T
                            t = s - 2
                            if j == 7 and 0 <= t < T:
                                act.wait_ge(norm_ready[0], n0 + (t + 1))
                                if t:
                                    act.wait_ge(sum2_done, n0 + t)
                                nc.scalar.activation(ln_o[:, :], y[:, t % 2, :], ACT.Identity, bias=norm[:, 0, 1:2],
                                                     scale=norm[:, 0, 0:1]).then_inc(ln_ready, 1)
                            t = s - 3
                            if j == 5 and 0 <= t < T:
                                act.wait_ge(norm_ready[1], n0 + (t + 1))
                                nc.scalar.activation(x_res[:, t % 2, :], x_res[:, t % 2, :], ACT.Identity,
                                                     bias=norm[:, 1, 1:2], scale=norm[:, 1, 0:1]).then_inc(out_ready, 1)

            bodies(act, body)

        @block.vector
        def _(dve):
            for t in range(T):
                dve.wait_ge(adj_loaded[t % 2], 16 * (t // 2 + 1))
                nc.vector.tensor_scalar(mask_q[:, t, :], adj_in[:, t % 2, :], 0.0, NEG, ALU.is_equal, ALU.mult
                                        ).then_inc(mask_q_ready, 1)
            for kc in range(KC):
                dve.wait_ge(w_hi_ready, kc + 1)
                nc.vector.scalar_tensor_tensor(w_lo[:, kc, :], w_in[:, kc, :], WSCALE, w_hi[:, kc, :],
                                               ALU.mult, ALU.subtract).then_inc(w_ready, 2)
            for kc in range(KC):
                dve.wait_ge(w_hi_ready, KC + kc + 1)
                nc.vector.scalar_tensor_tensor(wp_lo[:, kc, :], wp_in[:, kc, :], WSCALE, wp_hi[:, kc, :],
                                               ALU.mult, ALU.subtract).then_inc(w_ready, 2)
            dve.wait_ge(w_ready, 4 * KC)
            dve.wait_ge(mask_q_ready, T)
            for sl in range(2):
                nc.vector.memset(stack[HD:P, sl, :, K_B:K_B + 1, :], 0.0).then_inc(constants_set, 1)
                nc.vector.memset(stack[HD:P, sl, :, Q_B:Q_B + 1, :], 0.0).then_inc(constants_set, 1)
            dve.wait_ge(constants_set, 4)
            for sl in range(2):
                nc.vector.memset(stack[HD:HD + 2, sl, :, K_B:K_B + 1, :], 1.0).then_inc(constants_set, 1)

            def side_out(b, turn):
                kind, idx, whose = turn
                if kind == "PJ":
                    return
                bank = side[parity(b, turn)]
                dve.wait_ge(side_act, plus(turn_numbers(b, False)[turn], 1))
                if kind == "XT":
                    at = slice(idx * P, (idx + 1) * P)
                    nc.vector.tensor_tensor(xt_lo[:, :, at], bank[:, :].rearrange("p (k q) -> p k q", k=KC),
                                            xt_hi[:, :, at], ALU.subtract).then_inc(side_dve, 1)
                elif kind == "OT":
                    at = slice((idx % 2) * CH, (idx % 2 + 1) * CH)
                    nc.vector.tensor_tensor(ot_lo[:, idx // 2, at], bank[:, :], ot_hi[:, idx // 2, at],
                                            ALU.subtract).then_inc(side_dve, 1)
                elif kind == "QK":
                    nc.vector.scalar_tensor_tensor(qk_lo[:, idx % 4, :], bank[:, :], UNSCALE, qk_hi[:, idx % 4, :],
                                                   ALU.mult, ALU.subtract).then_inc(side_dve, 1)
                else:
                    heads = bank[:, :].rearrange("p (h d) -> p h d", h=H)
                    nc.vector.scalar_tensor_tensor(v_live[:, 0:H - 2, idx, HD + 1:VW], heads[:, 0:H - 2, :], UNSCALE,
                                                   v_live[:, 0:H - 2, idx, 0:HD], ALU.mult, ALU.subtract)
                    nc.vector.scalar_tensor_tensor(v_next[:, :, idx, HD + 1:VW], heads[:, H - 2:H, :], UNSCALE,
                                                   v_next[:, :, idx, 0:HD], ALU.mult, ALU.subtract
                                                   ).then_inc(side_dve, 1)

            def negate_c(b, s):
                tb, ts = row_target(b, s)
                if not is_batch(tb):
                    return
                m = ts % 2
                dve.wait_ge(max_done, tb * (STEPS * 4) + (ts + 1) * 4)
                wait(dve, c_row_ready, tb * STEPS + (ts - 1))
                nc.vector.tensor_scalar(c_neg[:, m, 0:4], c_max[:, m, :], -1.0, None, ALU.mult).then_inc(c_hi_done, 1)
                dve.wait_ge(c_hi_done, tb * STEPS + (ts + 1))
                nc.vector.scalar_tensor_tensor(c_neg[:, m, 4:8], c_max[:, m, :], -1.0, c_neg[:, m, 0:4],
                                               ALU.mult, ALU.subtract).then_inc(c_done, 1)

            def take_max(b, s, j):
                tb, ts = max_target(b, s)
                if not is_batch(tb):
                    return
                tile = j // 2
                qt = (ts % 2) * 4 + tile
                if tile == 0:
                    wait(dve, c_done, tb * STEPS + (ts - 1))
                wait_alone(dve, sm_ready, tb * (STEPS * 4) + (ts * 4 + tile + 1))
                nc.vector.tensor_tensor_reduce(out=sm_both[:, :], in0=sm_both[:, :], in1=mask_q[:, qt, :], scale=1.0,
                                               scalar=-3.0e38, op0=ALU.add, op1=ALU.max,
                                               accum_out=c_max[:, ts % 2, tile:tile + 1]).then_inc(max_done, 1)

            def normalise(b, s):
                ub, u = pv_unit(b, s, LAG - 1)
                if not is_batch(ub):
                    return
                us = u // SLOTS
                h, qc, pair = us // 2, us % 2, us // 4
                o = pv_bank[us % 2][:, 0:4 * (HD + 1)].rearrange("p (t w) -> p t w", t=4)
                dve.wait_ge(pv_done, ub * UNITS + (us + 1) * SLOTS)
                nc.vector.reciprocal(recip[:, us % 2, :].rearrange("p (t o) -> p t o", o=1), o[:, :, HD:HD + 1]
                                     ).then_inc(recip_done, 1)
                if us % 4 == 0:
                    if pair >= 2:
                        dve.wait_ge(side_ready, plus(turn_numbers(b, False)[("OT", 2 * pair - 3, CUR)], 1))
                    elif pair == 1 and active(b, PRV):
                        dve.wait_ge(side_ready, plus(turn_numbers(b, False)[("OT", 7, PRV)], 1))
                    elif pair == 0 and active(b, PRV):
                        dve.wait_ge(side_ready, plus(turn_numbers(b - 1, False)[("OT", 5, CUR)], 1))
                dve.wait_ge(recip_done, ub * STEPS + (us + 1))
                nc.vector.tensor_tensor(o_pair[:, pair % 2, qc * 4:qc * 4 + 4, (h % 2) * HD:(h % 2 + 1) * HD],
                                        o[:, :, 0:HD],
                                        recip[:, us % 2, :].rearrange("p (t o) -> p t o", o=1).broadcast_to([P, 4, HD]),
                                        ALU.mult).then_inc(o_done, 1)

            def norm_stats(which, src, done, scaled, n, part):
                if part == 0:
                    nc.vector.bn_stats(stats[:, which, :], src).then_inc(done, 1)
                elif part == 1:
                    wait_alone(dve, done, n * 3 + 1)
                    nc.vector.bn_aggr(mv[:, which, 0:2], stats[:, which, :]).then_inc(done, 1)
                elif part == 2:
                    dve.wait_ge(done, n * 3 + 2)
                    nc.vector.tensor_scalar(mv[:, which, 2:3], mv[:, which, 1:2], EPS, None, ALU.add).then_inc(done, 1)
                elif part == 4:
                    dve.wait_ge(scaled, n + 1)
                    nc.vector.tensor_scalar(norm[:, which, 1:2], mv[:, which, 0:1], norm[:, which, 0:1], -1.0,
                                            ALU.mult, ALU.mult).then_inc(norm_ready[which], 1)

            def body(b):
                for s in range(STEPS):
                    for j in range(SLOTS):
                        if j % 2:
                            take_max(b, s, j)
                        if active(b, CUR):
                            u = s * SLOTS + j
                            dve.wait_ge(exp16_done, b * UNITS + (u + 1))
                            nc.vector.tensor_tensor(p_lo[:, u % 4, :], p32[:, u % 4, :], p_hi[:, u % 4, :],
                                                    ALU.subtract).then_inc(lo_done, 1)
                        if j == LAG - 1:
                            normalise(b, s)
                        for turn in turns_ending(b, s, j):
                            side_out(b, turn)
                        if j == 0:
                            negate_c(b, s)
                        if active(b, PRV):
                            t = s - 2
                            n = b * T + (t - T)
                            if 0 <= t < T and 2 <= j < 7:
                                if j == 2:
                                    dve.wait_ge(o_biased, n + 1)
                                    if t:
                                        dve.wait_ge(ln_ready, n)
                                norm_stats(0, y[:, t % 2, :], stat_a, sigma_a, n, j - 2)
                            t = s - 3
                            n = b * T + (t - T)
                            if 0 <= t < T and j < 5:
                                if j == 0:
                                    dve.wait_ge(sum2_done, n + 1)
                                    if t:
                                        dve.wait_ge(out_ready, n)
                                norm_stats(1, x_res[:, t % 2, :], stat_b, sigma_b, n, j)

            bodies(dve, body)

        @block.gpsimd
        def _(pool):
            for m in (ident, ident_bf, ident_h):
                nc.gpsimd.memset(m[:, :], 0.0).then_inc(ident_zero, 1)
            pool.wait_ge(ident_zero, 3)
            for m in (ident, ident_bf, ident_h):
                nc.gpsimd.affine_select(out=m[:, :], in_=m[:, :], compare_op=ALU.not_equal, fill=1.0, base=0,
                                        pattern=[[-1, P]], channel_multiplier=1).then_inc(ident_ready, 1)
            for v in (v_live, v_next):
                nc.gpsimd.memset(v[:, :, :, :], 1.0).then_inc(ident_ready, 1)
            nc.gpsimd.memset(minus_half[:, :], -0.5).then_inc(half_set, 1)
            pool.wait_ge(half_set, 1)
            pool.wait_ge(const_loaded, 48)

            def body(b):
                if not active(b, PRV):
                    return

                def one_over_sigma(which, stat, scaled, t):
                    n = b * T + (t - T)
                    pool.wait_ge(stat, n * 3 + 3)
                    nc.gpsimd.tensor_tensor(norm[:, which, 0:1], mv[:, which, 2:3], minus_half[:, :], ALU.pow
                                            ).then_inc(scaled, 1)

                for t in range(T):
                    n = b * T + (t - T)
                    pool.wait_ge(side_act, plus(turn_numbers(b, False)[("PJ", t, PRV)], 1))
                    nc.gpsimd.tensor_tensor(y[:, t % 2, :], y[:, t % 2, :], bias_b[:, :], ALU.add).then_inc(o_biased, 1)
                    pool.wait_ge(xr_loaded[t % 2], b * 64 + (t // 2 * 16 - 64 + 16))
                    nc.gpsimd.tensor_tensor(x_res[:, t % 2, :], x_res[:, t % 2, :], beta_b[:, :], ALU.add
                                            ).then_inc(xr_biased, 1)
                    pool.wait_ge(o_biased, n + 1)
                    pool.wait_ge(xr_biased, n + 1)
                    nc.gpsimd.tensor_tensor(x_res[:, t % 2, :], x_res[:, t % 2, :], y[:, t % 2, :], ALU.add
                                            ).then_inc(sum1_done, 1)
                    if t:
                        one_over_sigma(1, stat_b, sigma_b, t - 1)
                    one_over_sigma(0, stat_a, sigma_a, t)
                    pool.wait_ge(ln_ready, n + 1)
                    nc.gpsimd.tensor_tensor(ln_o[:, :], ln_o[:, :], gamma_b[:, :], ALU.mult).then_inc(ln_scaled, 1)
                    pool.wait_ge(ln_scaled, n + 1)
                    pool.wait_ge(sum1_done, n + 1)
                    nc.gpsimd.tensor_tensor(x_res[:, t % 2, :], x_res[:, t % 2, :], ln_o[:, :], ALU.add
                                            ).then_inc(sum2_done, 1)
                one_over_sigma(1, stat_b, sigma_b, T - 1)

            bodies(pool, body)


_INS = ["x", "adj", "L0_gnn_w_qkv", "L0_gnn_w_proj", "L0_gnn_b_proj", "L0_gnn_ln_gamma", "L0_gnn_ln_beta"]


def kernel(**inputs):
    import numpy as np
    import concourse.bacc as bacc
    from concourse.bass_utils import run_bass_kernel_spmd

    nc = bacc.Bacc("TRN2", target_bir_lowering=False, num_devices=1)
    arrays, args = {}, []
    for name in _INS:
        a = np.ascontiguousarray(inputs[name])
        arrays[f"in_{name}"] = a
        args.append(nc.dram_tensor(f"in_{name}", a.shape, mybir.dt.from_np(a.dtype), kind="ExternalInput").ap())
    out = nc.dram_tensor("out_0", (B, N, D), F32, kind="ExternalOutput").ap()
    attention_block(nc, *args, out)
    r = run_bass_kernel_spmd(nc, [arrays], core_ids=[0])
    return r.results[0]["out_0"]
```

```python
from contextlib import ExitStack

import concourse.bass as bass
from concourse import mybir

F32, F16, BF16 = mybir.dt.float32, mybir.dt.float16, mybir.dt.bfloat16
ALU = mybir.AluOpType
ACT = mybir.ActivationFunctionType

P = 128
B, N, D, H = 16, 1024, 512, 8
HD = D // H
T = N // P
KC = D // P
CH = 512
STEPS = 2 * H
SLOTS = T
UNITS = STEPS * SLOTS
LAG = 3
MASK_SLOTS = {9: (), 10: (), 13: (0, 1, 2, 4, 5, 6), 14: (0, 1, 2, 4, 5, 6), 15: (0, 1, 2, 4, 5, 6)}
VECTOR_MASKS = tuple(s * SLOTS + j for s in range(STEPS) for j in MASK_SLOTS.get(s, (0, 2, 4, 6)))
VECTOR_LOWS = tuple(s * SLOTS + j for s in range(STEPS) for j in (1, 5))
POOL_LOWS = tuple(u for u in range(UNITS) if u not in VECTOR_LOWS)
VW = HD + 1 + HD
VP = VW + 1
WSCALE = 256.0
UNSCALE = 1.0 / WSCALE
SCALE = HD ** -0.5
NEG = -1.0e30
EPS = 1e-5
BIAS_LO = 32

NXT, CUR, PRV = "next", "current", "previous"
TURNS = {
    0: [("QK", 5, CUR), ("OT", 6, PRV), ("QK", 6, CUR), ("OT", 7, PRV)],
    1: [("QK", 7, CUR), ("PJ", 0, PRV)],
    2: [("PJ", 1, PRV), ("QK", 8, CUR)],
    3: [("PJ", 2, PRV), ("QK", 9, CUR)],
    4: [("PJ", 3, PRV), ("QK", 10, CUR)],
    5: [("PJ", 4, PRV), ("QK", 11, CUR)],
    6: [("PJ", 5, PRV), ("QK", 12, CUR)],
    7: [("PJ", 6, PRV), ("OT", 0, CUR), ("QK", 13, CUR)],
    8: [("PJ", 7, PRV), ("OT", 2, CUR), ("QK", 14, CUR), ("OT", 1, CUR)],
    9: [("QK", 15, CUR), ("XT", 0, NXT), ("XT", 1, NXT), ("XT", 2, NXT), ("XT", 3, NXT)],
    10: [("XT", t, NXT) for t in range(4, T)] + [("OT", 3, CUR)],
    11: [("QK", 0, NXT), ("QK", 1, NXT)],
    12: [("QK", 2, NXT), ("OT", 4, CUR), ("QK", 3, NXT), ("OT", 5, CUR)],
    13: [("V", 0, NXT), ("V", 1, NXT), ("V", 2, NXT)],
    14: [("V", 3, NXT), ("V", 4, NXT), ("V", 5, NXT)],
    15: [("V", 6, NXT), ("V", 7, NXT), ("QK", 4, NXT)],
}
STACK_AT = {0: [4], 1: [5, 6], 2: [7], 4: [8, 9], 5: [10], 6: [11], 8: [12, 13], 9: [14], 10: [15],
            12: [0, 1], 13: [2, 3]}
MATMULS = {"XT": KC, "OT": T // 2, "QK": 3 * KC, "V": 3 * KC, "PJ": 3 * KC + 1}


def active(b, whose):
    if not isinstance(b, int):
        return True
    return {NXT: b < B - 1, CUR: 0 <= b < B, PRV: b >= 1}[whose]


def turn_numbers(b, vector_only):
    def listed(body):
        return [t for s in range(STEPS) for t in TURNS[s]
                if active(body, t[2]) and not (vector_only and t[0] == "PJ")]
    if isinstance(b, int):
        before = sum(len(listed(x)) for x in range(-1, b))
    else:
        full = len([t for s in range(STEPS) for t in TURNS[s] if not (vector_only and t[0] == "PJ")])
        before = b * full + (len(listed(-1)) + len(listed(0)) - full)
    return {t: (before, i) for i, t in enumerate(listed(b))}


def plus(pair, k):
    return pair[0] + (pair[1] + k)


def parity(b, turn):
    if isinstance(b, int):
        before, i = turn_numbers(b, False)[turn]
        return (before + i) % 2
    before, i = turn_numbers(1, False)[turn]
    return (before + i) % 2


def slot_items(b, s, j):
    items = [(t, i) for t in TURNS[s] for i in range(MATMULS[t[0]])]
    n = len(items)
    return [(t, i) for t, i in items[n * j // SLOTS:n * (j + 1) // SLOTS] if active(b, t[2])]


def turns_ending(b, s, j):
    return [t for t, i in slot_items(b, s, j) if i == MATMULS[t[0]] - 1]


def owner(b, whose):
    return {NXT: b + 1, CUR: b, PRV: b - 1}[whose]


def wait(eng, sem, value):
    if isinstance(value, int) and value <= 0:
        return
    eng.wait_ge(sem, value)


def wait_alone(eng, sem, value):
    wait(eng, sem, value)
    eng.nop(nofuse=True)


def attention_block(nc, x, adj, w_qkv, w_proj, b_proj, gamma, beta, out):
    x_tiles = x.rearrange("b (t p) d -> (b t) p d", p=P)
    out_tiles = out.rearrange("b (t p) d -> (b t) p d", p=P)
    with ExitStack() as ctx:
        def sb(name, shape, dt):
            return ctx.enter_context(nc.sbuf_tensor(name, shape, dt))

        def sem(name):
            return ctx.enter_context(nc.semaphore(name))

        def sems(name, n):
            return [sem(f"{name}{i}") for i in range(n)]

        mask_q = sb("mask_q", [P, T, N], BF16)
        mask_k = sb("mask_k", [P, T, N], BF16)
        w_hi = sb("w_hi", [P, KC, 3 * D], F16)
        w_lo = sb("w_lo", [P, KC, 3 * D], F16)
        wp_hi = sb("wp_hi", [P, KC, D], F16)
        wp_lo = sb("wp_lo", [P, KC, D], F16)
        xt_hi = sb("xt_hi", [P, KC, N], F16)
        xt_lo = sb("xt_lo", [P, KC, N], F16)
        x_nat = sb("x_nat", [P, 4, D], F32)
        qk_hi = sb("qk_hi", [P, 4, CH], F16)
        qk_lo = sb("qk_lo", [P, 4, CH], F16)
        stack = sb("stack", [P, 2, 2, 4, N], F16)
        K_A, K_B, Q_A, Q_B = range(4)
        v_live = sb("v_live", [P, H, T, VP], F16)
        v_next = sb("v_next", [P, 2, T, VP], F16)
        p32 = sb("p32", [P, 4, CH], F32)
        p_hi = sb("p_hi", [P, 4, CH], F16)
        p_lo = sb("p_lo", [P, 4, CH], F16)
        o_pair = sb("o_pair", [P, 2, T, P], F32)
        ot_hi = sb("ot_hi", [P, KC, N], F16)
        ot_lo = sb("ot_lo", [P, KC, N], F16)
        c_max = sb("c_max", [P, 2, 4], F32)
        c_neg = sb("c_neg", [P, 2, 8], F16)
        c_row = sb("c_row", [8, 2, P], F16)
        recip = sb("recip", [P, 2, 4], F32)
        x_res = sb("x_res", [P, 2, D], F32)
        y = sb("y", [P, 2, D], F32)
        ln_o = sb("ln_o", [P, D], F32)
        stats = sb("stats", [P, 2, 6], F32)
        mv = sb("mv", [P, 2, 3], F32)
        norm = sb("norm", [P, 2, 2], F32)
        minus_half = sb("minus_half", [P, 1], F32)
        gamma_b = sb("gamma_b", [P, D], F32)
        beta_b = sb("beta_b", [P, D], F32)
        ones = sb("ones", [P, P], F16)
        bias_rows = sb("bias_rows", [P, D], F16)
        ident = sb("ident", [P, P], F32)
        ident_bf = sb("ident_bf", [P, P], BF16)
        ident_h = sb("ident_h", [P, P], F16)
        staging = stack[:, :, :, :, :].rearrange("p a b c n -> p (a b c n)").bitcast(F32)
        w_in = staging[:, 0:KC * 3 * D].rearrange("p (k n) -> p k n", k=KC)
        wp_in = ot_lo[:, :, :].rearrange("p k n -> p (k n)").bitcast(F32).rearrange("p (k n) -> p k n", k=KC)
        adj_in = o_pair[:, :, :, :].rearrange("p a t n -> p a (t n)")

        def pb(name):
            return ctx.enter_context(nc.psum_tensor(name, [P, CH], F32))

        st_bank = [pb(f"st_bank{i}") for i in range(2)]
        sm_both = ctx.enter_context(nc.psum_tensor("sm_both", [P, 2 * CH], F32))
        pv_bank = [pb(f"pv_bank{i}") for i in range(2)]
        side = [pb(f"side{i}") for i in range(2)]

        w_loaded, wp_loaded, const_loaded = sem("w_loaded"), sem("wp_loaded"), sem("const_loaded")
        adj_loaded = sems("adj_loaded", 2)
        ident_zero, ident_ready, constants_set = sem("ident_zero"), sem("ident_ready"), sem("constants_set")
        half_set, bias_ready, bias_zero = sem("half_set"), sem("bias_ready"), sem("bias_zero")
        w_hi_ready, w_ready = sem("w_hi_ready"), sem("w_ready")
        mask_q_ready, mask_t_ready, mask_k_ready = sem("mask_q_ready"), sem("mask_t_ready"), sem("mask_k_ready")
        x_loaded = sems("x_loaded", 4)
        k_in = sems("k_in", 2)
        q_in = [sems(f"q_in{i}_", 2) for i in range(2)]
        c_in = sems("c_in", 2)
        v_in = sems("v_in", 2)
        st_ready = sem("st_ready")
        exp16_done = sem("exp16_done")
        masked = sem("masked")
        lo_vector, lo_pool = sem("lo_vector"), sem("lo_pool")
        pv_done = sem("pv_done")
        o_done = sem("o_done")
        recip_done = sem("recip_done")
        sm_ready, max_done = sem("sm_ready"), sem("max_done")
        c_hi_done, c_done, ct_ready, c_row_ready = sem("c_hi_done"), sem("c_done"), sem("ct_ready"), sem("c_row_ready")
        side_ready, side_act, side_dve = sem("side_ready"), sem("side_act"), sem("side_dve")
        tail_loaded = sems("tail_loaded", T)
        xr_loaded, stored = sems("xr_loaded", 2), sems("stored", 2)
        xr_biased, sum1_done, ln_scaled, sum2_done = (
            sem("xr_biased"), sem("sum1_done"), sem("ln_scaled"), sem("sum2_done"))
        stat_a, stat_b = sem("stat_a"), sem("stat_b")
        sigma_a, sigma_b = sem("sigma_a"), sem("sigma_b")
        norm_ready = sems("norm_ready", 2)
        ln_ready, out_ready = sem("ln_ready"), sem("out_ready")

        block = ctx.enter_context(nc.Block())

        def bodies(eng, body):
            body(-1)
            body(0)
            with eng.Fori(1, B - 1) as b:
                body(b)
            body(B - 1)
            body(B)

        def first(b):
            return isinstance(b, int) and b < 0

        def last(b):
            return isinstance(b, int) and b == B

        def residual(b, t):
            if last(b):
                return x_nat[:, t, :] if t < 4 else p32[:, t - 4, :]
            return x_res[:, t % 2, :]

        def fills(batch, pair):
            return batch * 2 + (pair // 2 + 1)

        def max_target(b, s):
            return (b, s + 2) if s + 2 < STEPS else (b + 1, s + 2 - STEPS)

        def row_target(b, s):
            return (b, s + 1) if s + 1 < STEPS else (b + 1, 0)

        def is_batch(b):
            return not isinstance(b, int) or 0 <= b < B

        def unit_before(b, s, j, back):
            k = s * SLOTS + j - back
            return (b, k) if k >= 0 else (b - 1, k + UNITS)

        def pv_unit(b, s, j):
            return unit_before(b, s, j, LAG)

        def count_in(units, batch, u):
            return batch * len(units) + sum(k <= u for k in units)

        def wait_low(eng, batch, u):
            if not is_batch(batch):
                return
            if u in POOL_LOWS:
                eng.wait_ge(lo_pool, count_in(POOL_LOWS, batch, u))
            else:
                eng.wait_ge(lo_vector, count_in(VECTOR_LOWS, batch, u))

        @block.sync
        def _(sp):
            def load_x(b, t):
                if active(b, NXT):
                    if t >= 4:
                        wait_alone(sp, side_ready, plus(turn_numbers(b, False)[("XT", t - 4, NXT)], 1))
                    elif is_batch(b):
                        wait_alone(sp, side_ready, plus(turn_numbers(b - 1, False)[("XT", t + 4, NXT)], 1))
                    sp.dma_start(x_nat[:, t % 4, :], x_tiles[(b + 1) * T + t, :, :]).then_inc(x_loaded[t % 4], 16)

            for t in range(4):
                load_x(-1, t)
            for kc in range(KC):
                sp.dma_start(w_in[:, kc, :], w_qkv[kc * P:(kc + 1) * P, :]).then_inc(w_loaded, 16)
            for t in range(2):
                sp.dma_start(adj_in[:, t, :], adj[t * P:(t + 1) * P, :]).then_inc(adj_loaded[t], 16)
            for t in range(4, T):
                load_x(-1, t)
            for kc in range(KC):
                sp.dma_start(wp_in[:, kc, :], w_proj[kc * P:(kc + 1) * P, :]).then_inc(wp_loaded, 16)
            for dst, src in ((gamma_b, gamma), (beta_b, beta)):
                sp.dma_start(dst[:, :], src.rearrange("(o n) -> o n", o=1).broadcast_to([P, D])).then_inc(const_loaded, 16)
            for row in (0, BIAS_LO):
                sp.dma_start(ln_o[row:row + 1, :], b_proj.rearrange("(o n) -> o n", o=1)).then_inc(const_loaded, 16)
            for t in range(2, T):
                sp.wait_ge(mask_q_ready, t - 1)
                sp.dma_start(adj_in[:, t % 2, :], adj[t * P:(t + 1) * P, :]).then_inc(adj_loaded[t % 2], 16)

            def fill_stack(b, s, g):
                whose = NXT if g < 5 and s >= 11 else CUR
                turn = ("QK", g, NXT if g < 5 else CUR)
                made_in = b - 1 if g == 4 else b
                if not active(b, whose):
                    return
                batch = owner(b, whose)
                pair, part = g // 4, g % 4
                sl = pair % 2
                wait_alone(sp, side_dve, plus(turn_numbers(made_in, True)[turn], 1))
                wait(sp, st_ready, batch * UNITS + 32 * (pair - 1))
                for ph in range(2):
                    rows = slice(ph * HD, (ph + 1) * HD)
                    cols = slice((part % 2) * CH, (part % 2 + 1) * CH)
                    hi, lo = qk_hi[rows, g % 4, :], qk_lo[rows, g % 4, :]
                    if part < 2:
                        done = k_in[sl]
                        moves = ((K_A, 0, hi), (K_B, 0, hi), (K_A, HD, lo))
                    else:
                        done = q_in[sl][part % 2]
                        moves = ((Q_A, 0, hi), (Q_A, HD, hi), (Q_B, 0, lo))
                    for what, row, src in moves:
                        sp.dma_start(stack[row:row + HD, sl, ph, what, cols], src).then_inc(done, 16)

            def body(b):
                for s in range(STEPS):
                    for g in STACK_AT.get(s, ()):
                        fill_stack(b, s, g)
                    if s == 1 and is_batch(b):
                        sp.wait_ge(side_dve, plus(turn_numbers(b - 1, True)[("V", T - 1, NXT)], 1))
                        wait(sp, pv_done, b * UNITS)
                        for hh in range(2):
                            sp.dma_start(v_live[:, H - 2 + hh, :, :], v_next[:, hh, :, :]).then_inc(v_in[hh], 16)
                    if s == 12 and active(b, PRV):
                        for i in range(2):
                            wait_alone(sp, stored[i], b * 64)
                    if s == 12 and first(b):
                        sp.wait_ge(constants_set, 6)
                    if s == 0 and last(b):
                        for t in range(T):
                            if t == 4:
                                sp.wait_ge(pv_done, B * UNITS)
                            sp.dma_start(residual(b, t), x_tiles[(B - 1) * T + t, :, :]).then_inc(tail_loaded[t], 16)
                    if s == 6 and not first(b):
                        for t in range(4):
                            load_x(b, t)
                    for j in range(SLOTS):
                        for kind, t, whose in turns_ending(b, s, j):
                            if kind == "XT" and t < 4 and not first(b):
                                load_x(b, t + 4)
                        tb, ts = row_target(b, s)
                        if j == 4 and is_batch(tb):
                            h, qc = ts // 2, ts % 2
                            wait_alone(sp, c_row_ready, tb * STEPS + (ts + 1))
                            wait(sp, st_ready, tb * UNITS + (ts - 7) * SLOTS)
                            sp.dma_start(stack[HD:HD + 2, (h // 2) % 2, h % 2, Q_B, qc * CH:(qc + 1) * CH],
                                         c_row[:, ts % 2, :]).then_inc(c_in[ts % 2], 16)
                        if active(b, PRV):
                            n0 = b * T - T
                            t = s - 3
                            if j == 6 and 0 <= t < T:
                                wait_alone(sp, out_ready, n0 + (t + 1))
                                sp.dma_start(out_tiles[n0 + t, :, :], residual(b, t)).then_inc(stored[t % 2], 16)
                            t = s - 1
                            if j == 7 and 0 <= t < T and not last(b):
                                if t >= 2:
                                    wait_alone(sp, stored[t % 2], b * 64 + (t // 2 * 16 - 64))
                                sp.dma_start(x_res[:, t % 2, :], x_tiles[n0 + t, :, :]).then_inc(xr_loaded[t % 2], 16)

            bodies(sp, body)
            for i in range(2):
                sp.wait_ge(stored[i], 16 * B * T // 2)

        @block.tensor
        def _(pe):
            pe.wait_ge(ident_ready, 3)

            def transpose_mask(qt):
                pe.wait_ge(mask_q_ready, qt + 1)
                if qt >= 2:
                    pe.wait_ge(mask_k_ready, qt - 1)
                bank = st_bank[qt % 2][:, :].bitcast(BF16)
                for kt in range(T):
                    done = nc.tensor.transpose(bank[:, kt * P:(kt + 1) * P], mask_q[:, qt, kt * P:(kt + 1) * P],
                                               ident_bf[:, :])
                done.then_inc(mask_t_ready, 1)

            def side_matmul(b, turn, i):
                kind, idx, whose = turn
                bank = side[parity(b, turn)]
                batch = owner(b, whose)
                if i == 0:
                    number = turn_numbers(b, False)[turn]
                    wait(pe, side_act, plus(number, -1))
                    all_turns = list(turn_numbers(b, False))
                    at = all_turns.index(turn)
                    dve = turn_numbers(b, True)
                    before = len([t for t in all_turns[:at] if t[0] != "PJ"])
                    behind = 0 if at and all_turns[at - 1][0] == "PJ" else 1
                    base = next(iter(dve.values()))[0] if dve else 0
                    wait(pe, side_dve, base + (before - behind))
                k, part = min(i // 3, KC - 1), i % 3
                if kind == "XT":
                    if i == 0:
                        pe.wait_ge(x_loaded[idx % 4], batch * 32 + (idx // 4 + 1) * 16)
                    mm = nc.tensor.transpose(bank[:, i * P:(i + 1) * P], x_nat[:, idx % 4, i * P:(i + 1) * P], ident[:, :])
                elif kind == "OT":
                    pair, half = idx // 2, idx % 2
                    if i == 0:
                        pe.wait_ge(o_done, batch * STEPS + 4 * (pair + 1))
                    mm = nc.tensor.transpose(bank[:, i * P:(i + 1) * P], o_pair[:, pair % 2, half * 4 + i, :], ident[:, :])
                elif kind == "QK":
                    if i == 0 and idx == 0:
                        if first(b):
                            pe.wait_ge(w_ready, 2 * KC)
                        pe.wait_ge(side_dve, plus(turn_numbers(b, True)[("XT", T - 1, NXT)], 1))
                    g = idx % 4
                    col = (idx // 4) * P + (D if g < 2 else 0)
                    w = (w_hi, w_hi, w_lo)[part]
                    xt = (xt_hi, xt_lo, xt_hi)[part]
                    mm = nc.tensor.matmul(bank[:, :], w[:, k, col:col + P], xt[:, k, (g % 2) * CH:(g % 2 + 1) * CH],
                                          start=(i == 0), stop=(i == 3 * KC - 1))
                else:
                    if kind == "V":
                        rows, w, cols = (xt_hi, xt_lo, xt_hi)[part], (w_hi, w_hi, w_lo)[part], slice(2 * D, 3 * D)
                    else:
                        rows, w, cols = (ot_hi, ot_lo, ot_hi)[part], (wp_hi, wp_hi, wp_lo)[part], slice(0, D)
                        if i == 0 and idx == 0:
                            pe.wait_ge(side_dve, plus(turn_numbers(b, True)[("OT", 7, PRV)], 1))
                    if i < 3 * KC:
                        mm = nc.tensor.matmul(bank[:, :], rows[:, k, idx * P:(idx + 1) * P], w[:, k, cols],
                                              start=(i == 0), stop=(i == MATMULS[kind] - 1))
                    else:
                        mm = nc.tensor.matmul(bank[:, :], ones[:, :], bias_rows[:, :], start=False, stop=True)
                if i == MATMULS[kind] - 1:
                    mm.then_inc(side_ready, 1)

            def scores_t(b, s, j):
                h, qc, u = s // 2, s % 2, s * SLOTS + j
                q = slice(qc * CH, (qc + 1) * CH)
                keys = slice(j * P, (j + 1) * P)
                st = stack[:, (h // 2) % 2, h % 2, :, :]
                if j == 0:
                    pe.wait_ge(c_in[s % 2], b * (16 * 8) + (s // 2 + 1) * 16)
                bank = st_bank[j % 2]
                wait(pe, exp16_done, b * UNITS + (s * SLOTS + j - 1))
                nc.tensor.matmul(bank[:, :], st[:, K_A, keys], st[:, Q_A, q], start=True, stop=False)
                mm = nc.tensor.matmul(bank[:, :], st[:, K_B, keys], st[:, Q_B, q], start=False,
                                      stop=u in VECTOR_MASKS)
                if u not in VECTOR_MASKS:
                    mm = nc.tensor.matmul(bank[:, :], ident_bf[:, :], mask_k[:, j, q], start=False, stop=True)
                mm.then_inc(st_ready, 1)

            def times_v(b, s, j):
                ub, u = pv_unit(b, s, j)
                if not is_batch(ub):
                    return
                us, kt = u // SLOTS, u % SLOTS
                h = us // 2
                bank = pv_bank[us % 2]
                wait_low(pe, ub, u)
                if kt == 0:
                    wait(pe, o_done, ub * STEPS + (us - 1))
                    pe.wait_ge(c_row_ready, ub * STEPS + (us + 1))
                    if us == 0:
                        pe.wait_ge(side_dve, plus(turn_numbers(b - 1, True)[("V", T - 1, NXT)], 1))
                    if us in (2 * (H - 2), 2 * (H - 1)):
                        pe.wait_ge(v_in[h - (H - 2)], ub * 16 + 16)
                for t in range(4):
                    o = bank[:, t * (HD + 1):(t + 1) * (HD + 1)]
                    hi = p_hi[:, u % 4, t * P:(t + 1) * P]
                    lo = p_lo[:, u % 4, t * P:(t + 1) * P]
                    v = v_live[:, h, kt, :]
                    nc.tensor.matmul(o, hi, v[:, 0:HD + 1], start=(kt == 0 and t == 0), stop=False, skip_group_check=True)
                    nc.tensor.matmul(o[:, 0:HD], hi, v[:, HD + 1:VW], start=False, stop=False, skip_group_check=True)
                    mm = nc.tensor.matmul(o, lo, v[:, 0:HD + 1], start=False, stop=(kt == SLOTS - 1), skip_group_check=True)
                mm.then_inc(pv_done, 1)

            def scores_for_max(b, s, j):
                tb, ts = max_target(b, s)
                if not is_batch(tb):
                    return
                h, qc = ts // 2, ts % 2
                qt = qc * 4 + j // 2
                pair = h // 2
                if j == 0 and ts % 4 == 0:
                    pe.wait_ge(k_in[pair % 2], tb * (2 * 192) + (pair // 2 + 1) * 192)
                if j == 0 and ts % 4 < 2:
                    pe.wait_ge(q_in[pair % 2][qc], tb * (2 * 96) + (pair // 2 + 1) * 96)
                if j % 2 == 0:
                    wait(pe, max_done, tb * (STEPS * 4) + (ts * 4 + j // 2))
                st = stack[:, pair % 2, h % 2, :, :]
                mm = nc.tensor.matmul(sm_both[:, (j % 2) * CH:(j % 2 + 1) * CH], st[:, Q_A, qt * P:(qt + 1) * P],
                                      st[:, K_A, (j % 2) * CH:(j % 2 + 1) * CH], start=True, stop=True)
                if j % 2:
                    mm.then_inc(sm_ready, 1)

            def transpose_c(b, s):
                tb, ts = row_target(b, s)
                if not is_batch(tb):
                    return
                pe.wait_ge(c_done, tb * STEPS + (ts + 1))
                wait(pe, o_done, tb * STEPS + (ts - 1))
                nc.tensor.transpose(pv_bank[ts % 2][:, :].bitcast(F16)[0:8, 0:P], c_neg[:, ts % 2, :], ident_h[:, :]
                                    ).then_inc(ct_ready, 1)

            def body(b):
                for s in range(STEPS):
                    for j in range(SLOTS):
                        if first(b) and s == 12:
                            transpose_mask(j)
                        if isinstance(b, int) and (b, s, j) == (0, 0, 0):
                            pe.wait_ge(mask_k_ready, T)
                            pe.wait_ge(w_ready, 4 * KC)
                            pe.wait_ge(constants_set, 6)
                            pe.wait_ge(bias_ready, 4)
                        if j % 2:
                            scores_for_max(b, s, j)
                        if active(b, CUR):
                            scores_t(b, s, j)
                        times_v(b, s, j)
                        for turn, i in slot_items(b, s, j):
                            side_matmul(b, turn, i)
                        if j % 2 == 0:
                            scores_for_max(b, s, j)
                        if j == 4:
                            transpose_c(b, s)

            bodies(pe, body)

        @block.scalar
        def _(act):
            def prepare(s, j):
                if (s, j) == (11, 0):
                    act.wait_ge(w_loaded, 16 * KC)
                    for kc in range(KC):
                        nc.scalar.activation(w_hi[:, kc, :], w_in[:, kc, :], ACT.Copy, scale=WSCALE
                                             ).then_inc(w_hi_ready, 1)
                if s == 12:
                    act.wait_ge(mask_t_ready, j + 1)
                    nc.scalar.activation(mask_k[:, :, j * P:(j + 1) * P],
                                         st_bank[j % 2][:, :].bitcast(BF16).rearrange("p (k q) -> p k q", k=T),
                                         ACT.Copy).then_inc(mask_k_ready, 1)
                if s == 12 and j < KC:
                    act.wait_ge(wp_loaded, 16 * KC)
                    nc.scalar.activation(wp_hi[:, j, :], wp_in[:, j, :], ACT.Copy, scale=WSCALE).then_inc(w_hi_ready, 1)
                if (s, j) == (12, KC):
                    act.wait_ge(const_loaded, 64)
                    act.wait_ge(bias_zero, 1)
                    nc.scalar.activation(bias_rows[0:1, :], ln_o[0:1, :], ACT.Copy, scale=WSCALE
                                         ).then_inc(bias_ready, 1)
                    nc.scalar.activation(ot_hi[BIAS_LO:BIAS_LO + 1, 0, 0:D], ln_o[BIAS_LO:BIAS_LO + 1, :], ACT.Copy,
                                         scale=WSCALE).then_inc(bias_ready, 1)
                if (s, j) == (13, 0):
                    act.wait_ge(ident_ready, 5)

            def side_out(b, turn):
                kind, idx, whose = turn
                batch = owner(b, whose)
                bank = side[parity(b, turn)]
                act.wait_ge(side_ready, plus(turn_numbers(b, False)[turn], 1))
                if kind == "XT":
                    nc.scalar.activation(xt_hi[:, :, idx * P:(idx + 1) * P], bank[:, :].rearrange("p (k q) -> p k q", k=KC),
                                         ACT.Copy).then_inc(side_act, 1)
                elif kind == "OT":
                    nc.scalar.activation(ot_hi[:, idx // 2, (idx % 2) * CH:(idx % 2 + 1) * CH], bank[:, :],
                                         ACT.Copy).then_inc(side_act, 1)
                elif kind == "QK":
                    pair, part = idx // 4, idx % 4
                    sl = (pair + 1) % 2
                    filled = batch * 2 + (pair - 1) // 2 + 1 if pair else batch * 2
                    if part < 2:
                        wait(act, k_in[sl], filled * 192)
                    else:
                        wait(act, q_in[sl][part % 2], filled * 96)
                    nc.scalar.activation(qk_hi[:, idx % 4, :], bank[:, :], ACT.Copy, scale=UNSCALE).then_inc(side_act, 1)
                elif kind == "V":
                    heads = bank[:, :].rearrange("p (h d) -> p h d", h=H)
                    if idx == 0:
                        wait(act, pv_done, b * UNITS + (H - 2) * 2 * SLOTS)
                        for hh in range(2):
                            wait(act, v_in[hh], batch * 16)
                    nc.scalar.activation(v_live[:, 0:H - 2, idx, 0:HD], heads[:, 0:H - 2, :], ACT.Copy, scale=UNSCALE)
                    nc.scalar.activation(v_next[:, :, idx, 0:HD], heads[:, H - 2:H, :], ACT.Copy, scale=UNSCALE
                                         ).then_inc(side_act, 1)
                else:
                    if idx >= 2:
                        act.wait_ge(sum1_done, batch * T + (idx - 1))
                        act.wait_ge(ln_ready, batch * T + (idx - 1))
                    nc.scalar.activation(y[:, idx % 2, :], bank[:, :], ACT.Copy, scale=UNSCALE).then_inc(side_act, 1)

            def body(b):
                for s in range(STEPS):
                    for j in range(SLOTS):
                        if first(b):
                            prepare(s, j)
                        if active(b, CUR):
                            u = s * SLOTS + j
                            if u in VECTOR_MASKS:
                                act.wait_ge(masked, count_in(VECTOR_MASKS, b, u))
                            else:
                                act.wait_ge(st_ready, b * UNITS + (u + 1))
                            wait_low(act, *unit_before(b, s, j, 4))
                            nc.scalar.activation(p32[:, u % 4, :], st_bank[j % 2][:, :], ACT.Exp, scale=SCALE)
                            wait(act, pv_done, b * UNITS + (u - 3))
                            nc.scalar.activation(p_hi[:, u % 4, :], st_bank[j % 2][:, :], ACT.Exp, scale=SCALE
                                                 ).then_inc(exp16_done, 1)
                        for turn in turns_ending(b, s, j):
                            side_out(b, turn)
                        tb, ts = row_target(b, s)
                        if j == 4 and is_batch(tb):
                            act.wait_ge(ct_ready, tb * STEPS + (ts + 1))
                            wait(act, c_in[ts % 2], tb * (16 * 8) + (ts // 2) * 16)
                            nc.scalar.activation(c_row[:, ts % 2, :], pv_bank[ts % 2][:, :].bitcast(F16)[0:8, 0:P],
                                                 ACT.Copy).then_inc(c_row_ready, 1)
                        if active(b, PRV):
                            n0 = b * T - T
                            t = s - 2
                            if j == 5 and 0 <= t < T:
                                act.wait_ge(norm_ready[0], n0 + (t + 1))
                                if t:
                                    act.wait_ge(sum2_done, n0 + t)
                                nc.scalar.activation(ln_o[:, :], y[:, t % 2, :], ACT.Identity, bias=norm[:, 0, 1:2],
                                                     scale=norm[:, 0, 0:1]).then_inc(ln_ready, 1)
                            t = s - 3
                            if j == 5 and 0 <= t < T:
                                act.wait_ge(norm_ready[1], n0 + (t + 1))
                                nc.scalar.activation(residual(b, t), residual(b, t), ACT.Identity,
                                                     bias=norm[:, 1, 1:2], scale=norm[:, 1, 0:1]).then_inc(out_ready, 1)

            bodies(act, body)

        @block.vector
        def _(dve):
            nc.vector.memset(bias_rows[:, :], 0.0).then_inc(bias_zero, 1)
            nc.vector.memset(ones[:, :], 1.0).then_inc(bias_ready, 1)

            def prepare(s, j):
                if (s, j) == (11, 0):
                    for kc in range(KC):
                        dve.wait_ge(w_hi_ready, kc + 1)
                        nc.vector.scalar_tensor_tensor(w_lo[:, kc, :], w_in[:, kc, :], WSCALE, w_hi[:, kc, :],
                                                       ALU.mult, ALU.subtract).then_inc(w_ready, 2)
                if s == 11:
                    dve.wait_ge(adj_loaded[j % 2], 16 * (j // 2 + 1))
                    nc.vector.tensor_scalar(mask_q[:, j, :], adj_in[:, j % 2, :], 0.0, NEG, ALU.is_equal, ALU.mult
                                            ).then_inc(mask_q_ready, 1)
                if s == 12 and j < KC:
                    dve.wait_ge(w_hi_ready, KC + j + 1)
                    nc.vector.scalar_tensor_tensor(wp_lo[:, j, :], wp_in[:, j, :], WSCALE, wp_hi[:, j, :],
                                                   ALU.mult, ALU.subtract).then_inc(w_ready, 2)
                if (s, j) == (12, KC):
                    dve.wait_ge(bias_ready, 3)
                    nc.vector.scalar_tensor_tensor(bias_rows[BIAS_LO:BIAS_LO + 1, :], ln_o[BIAS_LO:BIAS_LO + 1, :],
                                                   WSCALE, ot_hi[BIAS_LO:BIAS_LO + 1, 0, 0:D], ALU.mult, ALU.subtract
                                                   ).then_inc(bias_ready, 1)

            def side_out(b, turn):
                kind, idx, whose = turn
                if kind == "PJ":
                    return
                bank = side[parity(b, turn)]
                dve.wait_ge(side_act, plus(turn_numbers(b, False)[turn], 1))
                if kind == "XT":
                    at = slice(idx * P, (idx + 1) * P)
                    nc.vector.tensor_tensor(xt_lo[:, :, at], bank[:, :].rearrange("p (k q) -> p k q", k=KC),
                                            xt_hi[:, :, at], ALU.subtract).then_inc(side_dve, 1)
                elif kind == "OT":
                    at = slice((idx % 2) * CH, (idx % 2 + 1) * CH)
                    nc.vector.tensor_tensor(ot_lo[:, idx // 2, at], bank[:, :], ot_hi[:, idx // 2, at],
                                            ALU.subtract).then_inc(side_dve, 1)
                elif kind == "QK":
                    nc.vector.scalar_tensor_tensor(qk_lo[:, idx % 4, :], bank[:, :], UNSCALE, qk_hi[:, idx % 4, :],
                                                   ALU.mult, ALU.subtract).then_inc(side_dve, 1)
                else:
                    heads = bank[:, :].rearrange("p (h d) -> p h d", h=H)
                    nc.vector.scalar_tensor_tensor(v_live[:, 0:H - 2, idx, HD + 1:VW], heads[:, 0:H - 2, :], UNSCALE,
                                                   v_live[:, 0:H - 2, idx, 0:HD], ALU.mult, ALU.subtract)
                    nc.vector.scalar_tensor_tensor(v_next[:, :, idx, HD + 1:VW], heads[:, H - 2:H, :], UNSCALE,
                                                   v_next[:, :, idx, 0:HD], ALU.mult, ALU.subtract
                                                   ).then_inc(side_dve, 1)

            def negate_c(b, s):
                tb, ts = row_target(b, s)
                if not is_batch(tb):
                    return
                m = ts % 2
                dve.wait_ge(max_done, tb * (STEPS * 4) + (ts + 1) * 4)
                wait(dve, c_row_ready, tb * STEPS + (ts - 1))
                nc.vector.tensor_scalar(c_neg[:, m, 0:4], c_max[:, m, :], -1.0, None, ALU.mult).then_inc(c_hi_done, 1)
                dve.wait_ge(c_hi_done, tb * STEPS + (ts + 1))
                nc.vector.scalar_tensor_tensor(c_neg[:, m, 4:8], c_max[:, m, :], -1.0, c_neg[:, m, 0:4],
                                               ALU.mult, ALU.subtract).then_inc(c_done, 1)

            def take_max(b, s, j):
                tb, ts = max_target(b, s)
                if not is_batch(tb):
                    return
                tile = j // 2
                qt = (ts % 2) * 4 + tile
                if tile == 0:
                    wait(dve, c_done, tb * STEPS + (ts - 1))
                wait_alone(dve, sm_ready, tb * (STEPS * 4) + (ts * 4 + tile + 1))
                nc.vector.tensor_tensor_reduce(out=sm_both[:, :], in0=sm_both[:, :], in1=mask_q[:, qt, :], scale=1.0,
                                               scalar=-3.0e38, op0=ALU.add, op1=ALU.max,
                                               accum_out=c_max[:, ts % 2, tile:tile + 1]).then_inc(max_done, 1)

            def normalise(b, s):
                ub, u = pv_unit(b, s, LAG - 1)
                if not is_batch(ub):
                    return
                us = u // SLOTS
                h, qc, pair = us // 2, us % 2, us // 4
                o = pv_bank[us % 2][:, 0:4 * (HD + 1)].rearrange("p (t w) -> p t w", t=4)
                dve.wait_ge(pv_done, ub * UNITS + (us + 1) * SLOTS)
                nc.vector.reciprocal(recip[:, us % 2, :].rearrange("p (t o) -> p t o", o=1), o[:, :, HD:HD + 1]
                                     ).then_inc(recip_done, 1)
                if us % 4 == 0:
                    if pair >= 2:
                        dve.wait_ge(side_ready, plus(turn_numbers(b, False)[("OT", 2 * pair - 3, CUR)], 1))
                    elif pair == 1 and active(b, PRV):
                        dve.wait_ge(side_ready, plus(turn_numbers(b, False)[("OT", 7, PRV)], 1))
                    elif pair == 0 and active(b, PRV):
                        dve.wait_ge(side_ready, plus(turn_numbers(b - 1, False)[("OT", 5, CUR)], 1))
                dve.wait_ge(recip_done, ub * STEPS + (us + 1))
                nc.vector.tensor_tensor(o_pair[:, pair % 2, qc * 4:qc * 4 + 4, (h % 2) * HD:(h % 2 + 1) * HD],
                                        o[:, :, 0:HD],
                                        recip[:, us % 2, :].rearrange("p (t o) -> p t o", o=1).broadcast_to([P, 4, HD]),
                                        ALU.mult).then_inc(o_done, 1)

            def norm_stats(which, src, done, scaled, n, part):
                if part == 0:
                    nc.vector.bn_stats(stats[:, which, :], src).then_inc(done, 1)
                elif part == 1:
                    wait_alone(dve, done, n * 3 + 1)
                    nc.vector.bn_aggr(mv[:, which, 0:2], stats[:, which, :]).then_inc(done, 1)
                elif part == 2:
                    dve.wait_ge(done, n * 3 + 2)
                    nc.vector.tensor_scalar(mv[:, which, 2:3], mv[:, which, 1:2], EPS, None, ALU.add).then_inc(done, 1)
                elif part == 4:
                    dve.wait_ge(scaled, n + 1)
                    nc.vector.tensor_scalar(norm[:, which, 1:2], mv[:, which, 0:1], norm[:, which, 0:1], -1.0,
                                            ALU.mult, ALU.mult).then_inc(norm_ready[which], 1)

            def body(b):
                for s in range(STEPS):
                    for j in range(SLOTS):
                        if first(b):
                            prepare(s, j)
                        if active(b, CUR):
                            u = s * SLOTS + j
                            if u in VECTOR_MASKS:
                                q = slice((s % 2) * CH, (s % 2 + 1) * CH)
                                dve.wait_ge(st_ready, b * UNITS + (u + 1))
                                nc.vector.tensor_tensor(st_bank[j % 2][:, :], st_bank[j % 2][:, :], mask_k[:, j, q],
                                                        ALU.add).then_inc(masked, 1)
                        if j % 2:
                            take_max(b, s, j)
                        if active(b, CUR) and j and s * SLOTS + j - 1 in VECTOR_LOWS:
                            u = s * SLOTS + j - 1
                            dve.wait_ge(exp16_done, b * UNITS + (u + 1))
                            nc.vector.tensor_tensor(p_lo[:, u % 4, :], p32[:, u % 4, :], p_hi[:, u % 4, :],
                                                    ALU.subtract).then_inc(lo_vector, 1)
                        if j == LAG - 1:
                            normalise(b, s)
                        for turn in turns_ending(b, s, j):
                            side_out(b, turn)
                        if j == 0:
                            negate_c(b, s)
                        if active(b, PRV):
                            t = s - 2
                            n = b * T + (t - T)
                            if 0 <= t < T and j < 5:
                                if j == 0:
                                    dve.wait_ge(side_act, plus(turn_numbers(b, False)[("PJ", t, PRV)], 1))
                                    if t:
                                        dve.wait_ge(ln_ready, n)
                                norm_stats(0, y[:, t % 2, :], stat_a, sigma_a, n, j)
                            t = s - 3
                            n = b * T + (t - T)
                            if 0 <= t < T and j < 5:
                                if j == 0:
                                    dve.wait_ge(sum2_done, n + 1)
                                    if t:
                                        dve.wait_ge(out_ready, n)
                                norm_stats(1, residual(b, t), stat_b, sigma_b, n, j)

            bodies(dve, body)

        @block.gpsimd
        def _(pool):
            for m in (ident, ident_bf, ident_h):
                nc.gpsimd.memset(m[:, :], 0.0).then_inc(ident_zero, 1)
            pool.wait_ge(ident_zero, 3)
            for m in (ident, ident_bf, ident_h):
                nc.gpsimd.affine_select(out=m[:, :], in_=m[:, :], compare_op=ALU.not_equal, fill=1.0, base=0,
                                        pattern=[[-1, P]], channel_multiplier=1).then_inc(ident_ready, 1)
            for v in (v_live, v_next):
                nc.gpsimd.memset(v[:, :, :, :], 1.0).then_inc(ident_ready, 1)
            nc.gpsimd.memset(minus_half[:, :], -0.5).then_inc(half_set, 1)
            pool.wait_ge(half_set, 1)
            pool.wait_ge(w_ready, 2 * KC)
            for sl in range(2):
                nc.gpsimd.memset(stack[HD:P, sl, :, K_B:K_B + 1, :], 0.0).then_inc(constants_set, 1)
                nc.gpsimd.memset(stack[HD:P, sl, :, Q_B:Q_B + 1, :], 0.0).then_inc(constants_set, 1)
            pool.wait_ge(constants_set, 4)
            for sl in range(2):
                nc.gpsimd.memset(stack[HD:HD + 2, sl, :, K_B:K_B + 1, :], 1.0).then_inc(constants_set, 1)
            pool.wait_ge(const_loaded, 64)

            def one_over_sigma(b, which, stat, scaled, t):
                n = b * T + (t - T)
                pool.wait_ge(stat, n * 3 + 3)
                nc.gpsimd.tensor_tensor(norm[:, which, 0:1], mv[:, which, 2:3], minus_half[:, :], ALU.pow
                                        ).then_inc(scaled, 1)

            def layer_norm_parts(b, s, j):
                t = s - 2
                n = b * T + (t - T)
                yt, xt = y[:, t % 2, :], residual(b, min(max(t, 0), T - 1))
                if 0 <= t < T and j == 1:
                    if last(b):
                        pool.wait_ge(tail_loaded[t], 16)
                    else:
                        pool.wait_ge(xr_loaded[t % 2], b * 64 + (t // 2 * 16 - 64 + 16))
                    nc.gpsimd.tensor_tensor(xt, xt, beta_b[:, :], ALU.add).then_inc(xr_biased, 1)
                if 0 <= t < T and j == 5:
                    pool.wait_ge(side_act, plus(turn_numbers(b, False)[("PJ", t, PRV)], 1))
                    pool.wait_ge(xr_biased, n + 1)
                    nc.gpsimd.tensor_tensor(xt, xt, yt, ALU.add).then_inc(sum1_done, 1)
                if 0 <= t < T and j == 3:
                    one_over_sigma(b, 0, stat_a, sigma_a, t)
                if 1 <= t <= T and j == 3:
                    one_over_sigma(b, 1, stat_b, sigma_b, t - 1)
                if 0 <= t < T and j == 6:
                    pool.wait_ge(ln_ready, n + 1)
                    nc.gpsimd.tensor_tensor(ln_o[:, :], ln_o[:, :], gamma_b[:, :], ALU.mult).then_inc(ln_scaled, 1)
                if 0 <= t < T and j == 7:
                    pool.wait_ge(ln_scaled, n + 1)
                    pool.wait_ge(sum1_done, n + 1)
                    nc.gpsimd.tensor_tensor(xt, xt, ln_o[:, :], ALU.add).then_inc(sum2_done, 1)

            def body(b):
                for s in range(STEPS):
                    for j in range(SLOTS):
                        if active(b, PRV):
                            layer_norm_parts(b, s, j)
                        if active(b, CUR) and s * SLOTS + j in POOL_LOWS:
                            u = s * SLOTS + j
                            pool.wait_ge(exp16_done, b * UNITS + (u + 1))
                            nc.gpsimd.tensor_tensor(p_lo[:, u % 4, :], p32[:, u % 4, :], p_hi[:, u % 4, :],
                                                    ALU.subtract).then_inc(lo_pool, 1)

            bodies(pool, body)


_INS = ["x", "adj", "L0_gnn_w_qkv", "L0_gnn_w_proj", "L0_gnn_b_proj", "L0_gnn_ln_gamma", "L0_gnn_ln_beta"]


def kernel(**inputs):
    import numpy as np
    import concourse.bacc as bacc
    from concourse.bass_utils import run_bass_kernel_spmd

    nc = bacc.Bacc("TRN2", target_bir_lowering=False, num_devices=1)
    arrays, args = {}, []
    for name in _INS:
        a = np.ascontiguousarray(inputs[name])
        arrays[f"in_{name}"] = a
        args.append(nc.dram_tensor(f"in_{name}", a.shape, mybir.dt.from_np(a.dtype), kind="ExternalInput").ap())
    out = nc.dram_tensor("out_0", (B, N, D), F32, kind="ExternalOutput").ap()
    attention_block(nc, *args, out)
    r = run_bass_kernel_spmd(nc, [arrays], core_ids=[0])
    return r.results[0]["out_0"]
```
